# Optimizing a Trainium2 kernel written in Bass

```python
import numpy as np
import jax
import jax.numpy as jnp

def _softmax(x, axis=-1):
    return jax.nn.softmax(x, axis=axis)

def _gelu(x):
    return jax.nn.gelu(x, approximate=True)

def _silu(x):
    return jax.nn.silu(x)

def _sigmoid(x):
    return jax.nn.sigmoid(x)

def _layernorm(x, axis=-1, eps=1e-05):
    m = jnp.mean(x, axis=axis, keepdims=True)
    v = jnp.var(x, axis=axis, keepdims=True)
    return (x - m) / jnp.sqrt(v + eps)

def _scatter_add(tgt, idx, src, axis=0):
    return tgt.at[idx].add(src)

def _segment_sum(src, seg, n):
    return jax.ops.segment_sum(src, seg, n)
kernel_name = 'mk_cond_resid_d2_seqx_r2_e0880e'

def setup_inputs(seed: int=0):
    np.random.seed(seed)
    _w = jnp.asarray

    def _rec_inputs():
        import jax
        import jax.numpy as jnp
        _rk = jax.random.key(seed)
        x = -0.000125 + 0.9999 * jax.random.normal(jax.random.fold_in(_rk, 1), (8, 512, 2048), jnp.float32)
        _lenS = 512 - jax.random.randint(jax.random.fold_in(_rk, 7), (8,), 0, max(1, 512 // 4) + 1, jnp.int32)
        _lenS2 = 512 - jax.random.randint(jax.random.fold_in(_rk, 8), (8,), 0, max(1, 512 // 4) + 1, jnp.int32)
        itok_B_6_15 = jax.random.randint(jax.random.fold_in(_rk, 11), (8,), 6, 16, jnp.int32)
        itok_B_3_7 = jax.random.randint(jax.random.fold_in(_rk, 12), (8,), 3, 8, jnp.int32)
        return (x, itok_B_6_15, itok_B_3_7)
    x, itok_B_6_15, itok_B_3_7 = _rec_inputs()

    def _L0_cond_setup():
        import jax, jax.numpy as jnp
        import numpy as np
        B, S, D_IN, D_OUT = (4, 1024, 2048, 2048)
        RANK, MAX_LORAS = (16, 32)
        key = jax.random.key(seed)
        ks = jax.random.split(key, 6)
        x = jax.random.normal(ks[0], (B, S, D_IN), dtype=jnp.float32)
        adapter_ids = jax.random.randint(ks[1], (B,), 0, MAX_LORAS)
        base_weight = jax.random.normal(ks[2], (D_OUT, D_IN), dtype=jnp.float32) * D_IN ** (-0.5)
        base_bias = jax.random.normal(ks[3], (D_OUT,), dtype=jnp.float32) * 0.01
        lora_A_w = jax.random.normal(ks[4], (MAX_LORAS, RANK, D_IN), dtype=jnp.float32) * D_IN ** (-0.5)
        lora_B_w = jax.random.normal(ks[5], (MAX_LORAS, D_OUT, RANK), dtype=jnp.float32) * RANK ** (-0.5)
        return {'x': x, 'adapter_ids': adapter_ids, 'base_weight': base_weight, 'base_bias': base_bias, 'lora_A_w': lora_A_w, 'lora_B_w': lora_B_w}
    _L0_cond_all = _L0_cond_setup()
    _L0_cond_in = {k: v for k, v in _L0_cond_all.items() if k in ('base_weight', 'base_bias', 'lora_A_w', 'lora_B_w')}
    del _L0_cond_all

    def _L1_cond_setup():
        import jax, jax.numpy as jnp
        import numpy as np
        MAX_LORAS, OUT, IN = (8, 2048, 2048)
        B, S = (4, 1024)
        key = jax.random.key(seed)
        k1, k2, k3 = jax.random.split(key, 3)
        x = jax.random.normal(k1, (B, S, IN), dtype=jnp.float32)
        weight = jax.random.normal(k2, (MAX_LORAS, OUT, IN), dtype=jnp.float32) * 0.02
        adapter_ids = jax.random.randint(k3, (B,), 0, MAX_LORAS, dtype=jnp.int32)
        return {'x': x, 'weight': weight, 'adapter_ids': adapter_ids}
    _L1_cond_all = _L1_cond_setup()
    _L1_cond_in = {k: v for k, v in _L1_cond_all.items() if k in ('weight',)}
    del _L1_cond_all
    return {'x': x, 'itok_B_6_15': itok_B_6_15, 'itok_B_3_7': itok_B_3_7, 'L0_cond_base_weight': _L0_cond_in['base_weight'], 'L0_cond_base_bias': _L0_cond_in['base_bias'], 'L0_cond_lora_A_w': _L0_cond_in['lora_A_w'], 'L0_cond_lora_B_w': _L0_cond_in['lora_B_w'], 'L1_cond_weight': _L1_cond_in['weight']}

def reference(x, itok_B_6_15, itok_B_3_7, L0_cond_base_weight, L0_cond_base_bias, L0_cond_lora_A_w, L0_cond_lora_B_w, L1_cond_weight):
    import jax
    import jax.numpy as jnp

    def _L0_cond_ref(x, adapter_ids, base_weight, base_bias, lora_A_w, lora_B_w):
        import jax, jax.numpy as jnp
        import numpy as np
        B, S, D_IN, D_OUT = (4, 1024, 2048, 2048)
        RANK, MAX_LORAS = (16, 32)
        result = jnp.einsum('bsd,od->bso', x, base_weight) + base_bias
        A = lora_A_w[adapter_ids]
        Bw = lora_B_w[adapter_ids]
        h = jnp.einsum('bsd,brd->bsr', x, A)
        lora_out = jnp.einsum('bsr,bor->bso', h, Bw)
        result = result + lora_out
        return result.astype(x.dtype)

    def _L1_cond_ref(x, weight, adapter_ids):
        import jax, jax.numpy as jnp
        import numpy as np
        MAX_LORAS, OUT, IN = (8, 2048, 2048)
        B, S = (4, 1024)
        w = weight[adapter_ids]
        return jnp.einsum('bsi,boi->bso', x, w)
    x = x + _L0_cond_ref(x, itok_B_6_15, L0_cond_base_weight, L0_cond_base_bias, L0_cond_lora_A_w, L0_cond_lora_B_w)
    x = x + _L1_cond_ref(x, L1_cond_weight, itok_B_3_7)
    return x

_drawn_inputs = setup_inputs


def setup_inputs(seed=0):
    import zlib

    import numpy as np

    out = dict(_drawn_inputs(seed))
    spreads = {}
    factors = {'L0_cond_base_bias': 8.0}
    for name, (base, spread) in spreads.items():
        noise = np.random.default_rng([zlib.crc32(name.encode()), seed]).standard_normal(out[name].shape)
        drawn = base * np.exp(spread * noise) if base else spread * noise
        out[name] = jnp.asarray(drawn.astype(out[name].dtype))
    for name, factor in factors.items():
        out[name] = (out[name] * factor).astype(out[name].dtype)
    return out
```

```python
from contextlib import ExitStack

import concourse.bass as bass
from concourse import mybir

F32 = mybir.dt.float32
F32R = mybir.dt.float32r
I32 = mybir.dt.int32
ALU = mybir.AluOpType
ACT = mybir.ActivationFunctionType

P = 128
S = 512
CW = 512
UK = 4


def cond_resid_kernel(nc, x_units, ids_lora, ids_weight, base_units, bias_cols, lora_a_cols, lora_b_rows,
                      weight_units, ident, out):
    NB = x_units.shape[0]
    NG = x_units.shape[1]
    D = NG * UK * P
    NC = D // CW
    NM = CW // P
    KT = NG * UK
    RANK = lora_b_rows.shape[1]
    N_LORA = lora_a_cols.shape[0]
    N_WEIGHT = weight_units.shape[0]
    UE = UK * CW
    UL = NC * NG
    UB = 2 * UL
    BL = NC * NM
    REP = P // (2 * RANK)
    Q = 2 * RANK

    with ExitStack() as ctx:
        def sb(name, shape, dt):
            return ctx.enter_context(nc.sbuf_tensor(name, shape, dt))

        def sem(name):
            return ctx.enter_context(nc.semaphore(name))

        x_hi = sb("x_hi", [P, KT, S], F32R)
        x_lo = sb("x_lo", [P, KT, S], F32R)
        y_hi = sb("y_hi", [P, KT, S], F32R)
        y_lo = sb("y_lo", [P, KT, S], F32R)
        w_hi = [sb(f"w_hi{i}", [P, UK, CW], F32R) for i in range(2)]
        w_lo = [sb(f"w_lo{i}", [P, UK, CW], F32R) for i in range(2)]
        w_in = [sb(f"w_in{i}", [P, UE], F32) for i in range(2)]
        x_in = sb("x_in", [P, UE], F32)
        a_in = sb("a_in", [P, KT, RANK], F32)
        a_cols = sb("a_cols", [P, KT, REP, 2 * RANK], F32R)
        b_in = sb("b_in", [P, CW], F32)
        b_rows = sb("b_rows", [P, CW], F32R)
        h_rows = sb("h_rows", [P, S], F32R)
        o_st = [sb(f"o_st{i}", [P, CW], F32) for i in range(2)]
        bias = sb("bias", [P, KT], F32)
        strip = sb("strip", [P, (2 * NG - 1) * P], F32)
        ids = sb("ids", [1, 2 * NB], I32)

        y_ps = [ctx.enter_context(nc.psum_tensor(f"y_ps{m}", [P, S], F32)) for m in range(NM)]
        o_ps = [ctx.enter_context(nc.psum_tensor(f"o_ps{m}", [P, CW], F32)) for m in range(NM)]
        h_ps = o_ps[0]

        ids_loaded = sem("ids_loaded")
        bias_loaded = sem("bias_loaded")
        ident_loaded = sem("ident_loaded")
        strip_zeroed = sem("strip_zeroed")
        w_loaded = [sem(f"w_loaded{i}") for i in range(2)]
        x_loaded = sem("x_loaded")
        a_loaded = sem("a_loaded")
        b_loaded = sem("b_loaded")
        w_plus_i = sem("w_plus_i")
        w_hi_done = sem("w_hi_done")
        w_lo_done = sem("w_lo_done")
        w_used = sem("w_used")
        x_hi_done = sem("x_hi_done")
        x_lo_done = sem("x_lo_done")
        a_hi_done = sem("a_hi_done")
        a_lo_done = sem("a_lo_done")
        b_hi_done = sem("b_hi_done")
        b_lo_done = sem("b_lo_done")
        h_summed = sem("h_summed")
        h_hi_done = sem("h_hi_done")
        h_lo_done = sem("h_lo_done")
        y_summed = sem("y_summed")
        y_hi_done = sem("y_hi_done")
        y_lo_done = sem("y_lo_done")
        o_summed = sem("o_summed")
        o_copied = sem("o_copied")
        o_stored = [sem(f"o_stored{i}") for i in range(2)]

        def unit0(b, c):
            return b * UB + c * NG

        def unit1(b, c):
            return b * UB + c * NG + UL

        def bank0(b, c):
            return b * BL + c * NM

        block = ctx.enter_context(nc.Block())

        @block.sync
        def _(sp):
            sp.dma_start(ids[0:1, 0:NB], ids_lora).then_inc(ids_loaded, 16)
            sp.dma_start(ids[0:1, NB:2 * NB], ids_weight).then_inc(ids_loaded, 16)
            sp.wait_ge(ids_loaded, 32)

            def load_x(b, g, first=False):
                if not first:
                    sp.wait_ge(x_lo_done, b * NG + g)
                sp.dma_start(x_in[:, :], x_units[bass.ds(b, 1), bass.ds(g, 1)].rearrange("b g p e -> (b g p) e")
                             ).then_inc(x_loaded, 16)

            def load_a(b, lora, first=False):
                if not first:
                    sp.wait_ge(a_lo_done, b)
                sp.dma_start(a_in[:, :, :].rearrange("p k r -> p (k r)"),
                             lora_a_cols[bass.ds(lora, 1)].rearrange("l p e -> (l p) e")).then_inc(a_loaded, 16)

            def load_b(b, c, lora, first=False):
                if not first:
                    sp.wait_ge(b_lo_done, b * NC + c)
                for i in range(P // RANK):
                    sp.dma_start(b_in[RANK * i:RANK * (i + 1), :],
                                 lora_b_rows[bass.ds(lora, 1), :, bass.ds(c * CW, CW)].rearrange("l r o -> (l r) o")
                                 ).then_inc(b_loaded, 16)

            def load_unit(u, g, src, first=False):
                if not first:
                    sp.wait_ge(w_lo_done, u + g - 1)
                sp.dma_start(w_in[g % 2][:, :], src).then_inc(w_loaded[g % 2], 16)

            def layer0_unit(c, g):
                return base_units[bass.ds(c, 1), g].rearrange("c p e -> (c p) e")

            def layer1_unit(weight, c, g):
                return weight_units[bass.ds(weight, 1), bass.ds(c, 1), g].rearrange("w c p e -> (w c p) e")

            lora = sp.value_load(ids[0:1, 0:1], min_val=0, max_val=N_LORA - 1)
            load_x(0, 0, first=True)
            load_unit(0, 0, layer0_unit(0, 0), first=True)
            load_a(0, lora, first=True)
            sp.dma_start(bias[:, :], bias_cols).then_inc(bias_loaded, 16)
            for g in range(1, NG):
                load_x(0, g)
            load_b(0, 0, lora, first=True)
            for g in range(1, NG):
                load_unit(0, g, layer0_unit(0, g), first=g < 2)
            with sp.Fori(1, NC) as c:
                load_b(0, c, lora)
                for g in range(NG):
                    load_unit(unit0(0, c), g, layer0_unit(c, g))

            with sp.Fori(1, NB) as b:
                lora_b = sp.value_load(ids[0:1, bass.ds(b, 1)], min_val=0, max_val=N_LORA - 1)
                weight = sp.value_load(ids[0:1, bass.ds(b + (NB - 1), 1)], min_val=0, max_val=N_WEIGHT - 1)
                load_a(b, lora_b)
                with sp.Fori(0, NC) as c:
                    for g in range(NG):
                        load_unit(unit1(b - 1, c), g, layer1_unit(weight, c, g))
                        if g == 1:
                            load_x(b, c)
                with sp.Fori(0, NC) as c:
                    load_b(b, c, lora_b)
                    for g in range(NG):
                        load_unit(unit0(b, c), g, layer0_unit(c, g))

            weight = sp.value_load(ids[0:1, 2 * NB - 1:2 * NB], min_val=0, max_val=N_WEIGHT - 1)
            with sp.Fori(0, NC) as c:
                for g in range(NG):
                    load_unit(unit1(NB - 1, c), g, layer1_unit(weight, c, g))

        @block.gpsimd
        def _(pool):
            mid = strip[:, (NG - 1) * P:NG * P]
            nc.gpsimd.memset(strip[:, :], 0.0).then_inc(strip_zeroed, 1)
            pool.wait_ge(strip_zeroed, 1)
            pool.dma_start(mid, ident).then_inc(ident_loaded, 16)
            pool.wait_ge(ident_loaded, 16)

            def add_identity(u, c, g):
                pool.wait_ge(w_loaded[g % 2], (u // 2) * 16 + (g // 2 + 1) * 16)
                w = w_in[g % 2][:, :]
                diagonal = bass.AP(w.tensor, w.offset, [w.ap[0], [CW + P, UK], [1, P]])
                block_of_strip = strip[:, bass.ds((c + (NG - 1 - g)) * P, P)].unsqueeze(1).broadcast_to([P, UK, P])
                nc.gpsimd.tensor_tensor(diagonal, diagonal, block_of_strip, ALU.add).then_inc(w_plus_i, 1)

            with pool.Fori(0, NB) as b:
                with pool.Fori(0, NC) as c:
                    for g in range(NG):
                        add_identity(unit0(b, c), c, g)
                with pool.Fori(0, NC) as c:
                    for g in range(NG):
                        add_identity(unit1(b, c), c, g)

        @block.scalar
        def _(act):
            def split_unit(u, g, first=False):
                act.wait_ge(w_plus_i, u + g + 1)
                if not first:
                    act.wait_ge(w_used, u + g - 1)
                nc.scalar.copy(w_hi[g % 2][:, :, :].rearrange("p k o -> p (k o)"), w_in[g % 2][:, :]
                               ).then_inc(w_hi_done, 1)

            def split_x(b, g, last_use):
                act.wait_ge(x_loaded, (b * NG + g + 1) * 16)
                if last_use is not None:
                    act.wait_ge(w_used, last_use)
                nc.scalar.copy(x_hi[:, bass.ds(g * UK, UK), :].rearrange("p k s -> p (k s)"), x_in[:, :]
                               ).then_inc(x_hi_done, 1)

            def split_a(b, first=False):
                act.wait_ge(a_loaded, (b + 1) * 16)
                if not first:
                    act.wait_ge(h_summed, b)
                nc.scalar.copy(a_cols[:, :, :, 0:RANK],
                               a_in[:, :, :].unsqueeze(2).broadcast_to([P, KT, REP, RANK])).then_inc(a_hi_done, 1)

            def split_b(b, c, first=False):
                act.wait_ge(b_loaded, (b * NC + c + 1) * (P // RANK * 16))
                if not first:
                    act.wait_ge(y_summed, bank0(b, c))
                nc.scalar.copy(b_rows[:, :], b_in[:, :]).then_inc(b_hi_done, 1)

            def split_h(b):
                act.wait_ge(h_summed, b + 1)
                nc.scalar.copy(h_rows[:, :], h_ps[:, :]).then_inc(h_hi_done, 1)

            def layer0_chunk(b, c, first=False):
                u = unit0(b, c)
                split_unit(u, 1, first)
                split_b(b, c, first)
                split_unit(u, 2)
                split_unit(u, 3)
                split_unit(u, 4)
                for m in range(NM):
                    act.wait_ge(y_summed, bank0(b, c) + m + 1)
                    nc.scalar.activation(y_hi[:, bass.ds(c * NM + m, 1), :].rearrange("p k s -> p (k s)"),
                                         y_ps[m][:, :], ACT.Identity, bias=bias[:, bass.ds(c * NM + m, 1)]
                                         ).then_inc(y_hi_done, 1)

            def layer1_chunk(b, c, next_x, last=False):
                u = unit1(b, c)
                split_unit(u, 1)
                if next_x:
                    split_x(b + 1, c, unit1(b, 0))
                split_unit(u, 2)
                split_unit(u, 3)
                if not last:
                    split_unit(u, 4)
                for m in range(NM):
                    n = bank0(b, c) + m
                    act.wait_ge(o_copied, n + 1)
                    act.dma_start(out[bass.ds(b, 1), m * P:(m + 1) * P, bass.ds(c * CW, CW)].rearrange(
                        "b s o -> (b s) o"), o_st[m % 2][:, :]).then_inc(o_stored[m % 2], 16)

            act.wait_ge(bias_loaded, 16)
            split_x(0, 0, None)
            split_unit(0, 0, first=True)
            split_a(0, first=True)
            for g in range(1, NG):
                split_x(0, g, None)
            split_h(0)
            layer0_chunk(0, 0, first=True)
            with act.Fori(1, NC) as c:
                layer0_chunk(0, c)
            with act.Fori(1, NB) as b:
                split_a(b)
                with act.Fori(0, NC) as c:
                    layer1_chunk(b - 1, c, True)
                split_h(b)
                with act.Fori(0, NC) as c:
                    layer0_chunk(b, c)
            with act.Fori(0, NC - 1) as c:
                layer1_chunk(NB - 1, c, False)
            layer1_chunk(NB - 1, NC - 1, False, last=True)
            for i in range(2):
                act.wait_ge(o_stored[i], 16 * NB * BL // 2)

        @block.vector
        def _(dve):
            def split_unit(u, g):
                dve.wait_ge(w_hi_done, u + g + 1)
                flat = "p k o -> p (k o)"
                nc.vector.tensor_tensor(w_lo[g % 2][:, :, :].rearrange(flat), w_in[g % 2][:, :],
                                        w_hi[g % 2][:, :, :].rearrange(flat).bitcast(F32), ALU.subtract
                                        ).then_inc(w_lo_done, 1)

            def split_x(b, g):
                dve.wait_ge(x_hi_done, b * NG + g + 1)
                flat = "p k s -> p (k s)"
                nc.vector.tensor_tensor(x_lo[:, bass.ds(g * UK, UK), :].rearrange(flat), x_in[:, :],
                                        x_hi[:, bass.ds(g * UK, UK), :].rearrange(flat).bitcast(F32), ALU.subtract
                                        ).then_inc(x_lo_done, 1)

            def split_a(b):
                dve.wait_ge(a_hi_done, b + 1)
                nc.vector.tensor_tensor(a_cols[:, :, :, RANK:2 * RANK],
                                        a_in[:, :, :].unsqueeze(2).broadcast_to([P, KT, REP, RANK]),
                                        a_cols[:, :, :, 0:RANK].bitcast(F32), ALU.subtract).then_inc(a_lo_done, 1)

            def split_b(b, c):
                dve.wait_ge(b_hi_done, b * NC + c + 1)
                nc.vector.tensor_tensor(b_rows[P // 2:P, :], b_in[P // 2:P, :], b_rows[P // 2:P, :].bitcast(F32),
                                        ALU.subtract).then_inc(b_lo_done, 1)

            def split_h(b):
                dve.wait_ge(h_hi_done, b + 1)
                for q in (1, 3):
                    rows = slice(q * Q, (q + 1) * Q)
                    nc.vector.tensor_tensor(h_rows[rows, :], h_ps[rows, :], h_rows[rows, :].bitcast(F32),
                                            ALU.subtract).then_inc(h_lo_done, 1)

            def layer0_chunk(b, c):
                u = unit0(b, c)
                split_unit(u, 1)
                split_b(b, c)
                split_unit(u, 2)
                split_unit(u, 3)
                split_unit(u, 4)
                for m in range(NM):
                    dve.wait_ge(y_hi_done, bank0(b, c) + m + 1)
                    k = bass.ds(c * NM + m, 1)
                    flat = "p k s -> p (k s)"
                    nc.vector.scalar_tensor_tensor(y_lo[:, k, :].rearrange(flat), y_ps[m][:, :], bias[:, k],
                                                   y_hi[:, k, :].rearrange(flat).bitcast(F32), ALU.add, ALU.subtract
                                                   ).then_inc(y_lo_done, 1)

            def layer1_chunk(b, c, next_x, last=False, first=False):
                u = unit1(b, c)
                split_unit(u, 1)
                if next_x:
                    split_x(b + 1, c)
                split_unit(u, 2)
                split_unit(u, 3)
                if not last:
                    split_unit(u, 4)
                for m in range(NM):
                    n = bank0(b, c) + m
                    if m < NM - 1:
                        dve.wait_ge(o_summed, (b * NC + c) * (NM - 1) + m + 1)
                    else:
                        dve.wait_ge(w_used, u + NG)
                    if not (first and m < 2):
                        dve.wait_ge(o_stored[m % 2], (bank0(b, c) // 2 + m // 2) * 16)
                    nc.vector.tensor_copy(o_st[m % 2][:, :], o_ps[m][:, :]).then_inc(o_copied, 1)

            dve.wait_ge(bias_loaded, 16)
            split_x(0, 0)
            split_unit(0, 0)
            split_a(0)
            for g in range(1, NG):
                split_x(0, g)
            split_h(0)
            with dve.Fori(0, NC) as c:
                layer0_chunk(0, c)
            split_a(1)
            layer1_chunk(0, 0, True, first=True)
            with dve.Fori(1, NC) as c:
                layer1_chunk(0, c, True)
            with dve.Fori(1, NB - 1) as b:
                split_h(b)
                with dve.Fori(0, NC) as c:
                    layer0_chunk(b, c)
                split_a(b + 1)
                with dve.Fori(0, NC) as c:
                    layer1_chunk(b, c, True)
            split_h(NB - 1)
            with dve.Fori(0, NC) as c:
                layer0_chunk(NB - 1, c)
            with dve.Fori(0, NC - 1) as c:
                layer1_chunk(NB - 1, c, False)
            layer1_chunk(NB - 1, NC - 1, False, last=True)

        @block.tensor
        def _(pe):
            def make_h(b, first=False):
                if not first:
                    pe.wait_ge(o_copied, bank0(b - 1, NC - 1) + 1)
                pe.wait_ge(a_hi_done, b + 1)
                pe.wait_ge(a_lo_done, b + 1)
                for k in range(KT):
                    if k % UK == 0:
                        pe.wait_ge(x_hi_done, b * NG + k // UK + 1)
                        pe.wait_ge(x_lo_done, b * NG + k // UK + 1)
                    a = a_cols[:, k, :, :].rearrange("p q r -> p (q r)")
                    nc.tensor.matmul(h_ps[:, :], a, x_hi[:, k, :], start=(k == 0), stop=False)
                    mm = nc.tensor.matmul(h_ps[:, :], a, x_lo[:, k, :], start=False, stop=(k == KT - 1))
                mm.then_inc(h_summed, 1)

            def wait_unit(u, g):
                pe.wait_ge(w_hi_done, u + g + 1)
                pe.wait_ge(w_lo_done, u + g + 1)

            def layer0_chunk(b, c, first=False):
                for g in range(NG):
                    wait_unit(unit0(b, c), g)
                    wh, wl = w_hi[g % 2], w_lo[g % 2]
                    for m in range(NM):
                        if g == 0 and not first:
                            pe.wait_ge(y_lo_done, bank0(b, c) - NM + m + 1)
                        o = slice(m * P, (m + 1) * P)
                        for r in range(UK):
                            k = g * UK + r
                            nc.tensor.matmul(y_ps[m][:, :], wh[:, r, o], x_hi[:, k, :], start=(k == 0), stop=False)
                            nc.tensor.matmul(y_ps[m][:, :], wh[:, r, o], x_lo[:, k, :], start=False, stop=False)
                            mm = nc.tensor.matmul(y_ps[m][:, :], wl[:, r, o], x_hi[:, k, :], start=False, stop=False)
                        if g == NG - 1:
                            if m == 0:
                                pe.wait_ge(h_hi_done, b + 1)
                                pe.wait_ge(h_lo_done, (b + 1) * 2)
                                pe.wait_ge(b_hi_done, b * NC + c + 1)
                                pe.wait_ge(b_lo_done, b * NC + c + 1)
                            nc.tensor.matmul(y_ps[m][:, :], b_rows[:, o], h_rows[:, :], start=False, stop=True
                                             ).then_inc(y_summed, 1)
                    mm.then_inc(w_used, 1)

            def layer1_chunk(b, c, first=False):
                for g in range(NG):
                    wait_unit(unit1(b, c), g)
                    pe.wait_ge(y_hi_done, bank0(b, 0) + (g + 1) * NM)
                    pe.wait_ge(y_lo_done, bank0(b, 0) + (g + 1) * NM)
                    wh, wl = w_hi[g % 2], w_lo[g % 2]
                    for m in range(NM):
                        if g == 0 and not first:
                            pe.wait_ge(o_copied, bank0(b, c) - NM + m + 1)
                        s = slice(m * P, (m + 1) * P)
                        for r in range(UK):
                            k = g * UK + r
                            nc.tensor.matmul(o_ps[m][:, :], y_hi[:, k, s], wh[:, r, :], start=(k == 0), stop=False)
                            nc.tensor.matmul(o_ps[m][:, :], y_hi[:, k, s], wl[:, r, :], start=False, stop=False)
                            mm = nc.tensor.matmul(o_ps[m][:, :], y_lo[:, k, s], wh[:, r, :], start=False,
                                                  stop=(k == KT - 1))
                        if g == NG - 1 and m < NM - 1:
                            mm.then_inc(o_summed, 1)
                    mm.then_inc(w_used, 1)

            make_h(0, first=True)
            layer0_chunk(0, 0, first=True)
            with pe.Fori(1, NC) as c:
                layer0_chunk(0, c)
            layer1_chunk(0, 0, first=True)
            with pe.Fori(1, NC) as c:
                layer1_chunk(0, c)
            with pe.Fori(1, NB) as b:
                make_h(b)
                with pe.Fori(0, NC) as c:
                    layer0_chunk(b, c)
                with pe.Fori(0, NC) as c:
                    layer1_chunk(b, c)


def kernel(**inputs):
    import numpy as np
    import concourse.bacc as bacc
    from concourse.bass_utils import run_bass_kernel_spmd

    a = {name: np.asarray(value) for name, value in inputs.items()}
    x, base, weight = a["x"], a["L0_cond_base_weight"], a["L1_cond_weight"]
    lora_a, lora_b = a["L0_cond_lora_A_w"], a["L0_cond_lora_B_w"]
    nb, s, d = x.shape
    ng, nc_, kt = d // (P * UK), d // CW, d // P

    def weight_layout(w):
        w = w.reshape(*w.shape[:-2], nc_, CW, ng, UK, P)
        n = w.ndim
        w = w.transpose(*range(n - 5), n - 5, n - 3, n - 1, n - 2, n - 4)
        return np.ascontiguousarray(w).reshape(*w.shape[:-2], UK * CW)

    arrays = {
        "x_units": np.ascontiguousarray(x.reshape(nb, s, ng, UK, P).transpose(0, 2, 4, 3, 1)).reshape(nb, ng, P, UK * s),
        "ids_lora": a["itok_B_6_15"].reshape(1, nb),
        "ids_weight": a["itok_B_3_7"].reshape(1, nb),
        "base_units": weight_layout(base),
        "bias_cols": np.ascontiguousarray(a["L0_cond_base_bias"].reshape(kt, P).T),
        "lora_a_cols": np.ascontiguousarray(lora_a.reshape(*lora_a.shape[:2], kt, P).transpose(0, 3, 2, 1)).reshape(
            lora_a.shape[0], P, -1),
        "lora_b_rows": np.ascontiguousarray(lora_b.transpose(0, 2, 1)),
        "weight_units": weight_layout(weight),
        "ident": np.eye(P, dtype=np.float32),
    }
    nc = bacc.Bacc("TRN2", target_bir_lowering=False, num_devices=1)
    args = [nc.dram_tensor(f"in_{k}", v.shape, mybir.dt.from_np(v.dtype), kind="ExternalInput").ap()
            for k, v in arrays.items()]
    out = nc.dram_tensor("out_y", (nb, s, d), F32, kind="ExternalOutput").ap()
    cond_resid_kernel(nc, *args, out)
    r = run_bass_kernel_spmd(nc, [{f"in_{k}": v for k, v in arrays.items()}], core_ids=[0])
    return r.results[0]["out_y"]
```

```python
from contextlib import ExitStack

import concourse.bass as bass
from concourse import mybir

F32 = mybir.dt.float32
F32R = mybir.dt.float32r
I32 = mybir.dt.int32
ALU = mybir.AluOpType
ACT = mybir.ActivationFunctionType

P = 128
S = 512
CW = 512
UK = 4


def cond_resid_kernel(nc, x_units, ids_lora, ids_weight, base_units, bias_cols, lora_a_cols, lora_b_rows,
                      weight_units, ident, out):
    NB = x_units.shape[0]
    NG = x_units.shape[1]
    D = NG * UK * P
    NC = D // CW
    NM = CW // P
    KT = NG * UK
    RANK = lora_b_rows.shape[1]
    N_LORA = lora_a_cols.shape[0]
    N_WEIGHT = weight_units.shape[0]
    UE = UK * CW
    UL = NC * NG
    UB = 2 * UL
    BL = NC * NM
    REP = P // (2 * RANK)
    Q = 2 * RANK

    with ExitStack() as ctx:
        def sb(name, shape, dt):
            return ctx.enter_context(nc.sbuf_tensor(name, shape, dt))

        def sem(name):
            return ctx.enter_context(nc.semaphore(name))

        x_hi = sb("x_hi", [P, KT, S], F32R)
        x_lo = sb("x_lo", [P, KT, S], F32R)
        y_hi = sb("y_hi", [P, KT, S], F32R)
        y_lo = sb("y_lo", [P, KT, S], F32R)
        w_hi = [sb(f"w_hi{i}", [P, UK, CW], F32R) for i in range(2)]
        w_lo = [sb(f"w_lo{i}", [P, UK, CW], F32R) for i in range(2)]
        w_in = [sb(f"w_in{i}", [P, UE], F32) for i in range(2)]
        x_in = sb("x_in", [P, UE], F32)
        a_in = sb("a_in", [P, KT, RANK], F32)
        a_cols = sb("a_cols", [P, KT, REP, 2 * RANK], F32R)
        b_in = sb("b_in", [P, CW], F32)
        b_rows = sb("b_rows", [P, CW], F32R)
        h_rows = sb("h_rows", [P, S], F32R)
        o_st = [sb(f"o_st{i}", [P, CW], F32) for i in range(2)]
        bias = sb("bias", [P, KT], F32)
        strip = sb("strip", [P, (2 * NG - 1) * P], F32)
        ids = sb("ids", [1, 2 * NB], I32)

        y_ps = [ctx.enter_context(nc.psum_tensor(f"y_ps{m}", [P, S], F32)) for m in range(NM)]
        o_ps = [ctx.enter_context(nc.psum_tensor(f"o_ps{m}", [P, CW], F32)) for m in range(NM)]
        h_ps = o_ps[0]

        ids_loaded = sem("ids_loaded")
        bias_loaded = sem("bias_loaded")
        ident_loaded = sem("ident_loaded")
        strip_zeroed = sem("strip_zeroed")
        w_loaded = [sem(f"w_loaded{i}") for i in range(2)]
        x_loaded = sem("x_loaded")
        w_part_loaded = [sem(f"w_part_loaded{r}") for r in range(UK - 1)]
        x_part_loaded = [sem(f"x_part_loaded{r}") for r in range(UK - 1)]
        w_part_plus_i = sem("w_part_plus_i")
        w_part_hi_done = sem("w_part_hi_done")
        w_part_lo_done = sem("w_part_lo_done")
        x_part_hi_done = sem("x_part_hi_done")
        x_part_lo_done = sem("x_part_lo_done")
        a_loaded = sem("a_loaded")
        b_loaded = sem("b_loaded")
        w_plus_i = sem("w_plus_i")
        w_hi_done = sem("w_hi_done")
        w_lo_done = sem("w_lo_done")
        w_used = sem("w_used")
        x_hi_done = sem("x_hi_done")
        x_lo_done = sem("x_lo_done")
        a_hi_done = sem("a_hi_done")
        a_lo_done = sem("a_lo_done")
        b_hi_done = sem("b_hi_done")
        b_lo_done = sem("b_lo_done")
        h_summed = sem("h_summed")
        h_hi_done = sem("h_hi_done")
        h_lo_done = sem("h_lo_done")
        y_summed = sem("y_summed")
        y_hi_done = sem("y_hi_done")
        y_lo_done = sem("y_lo_done")
        o_summed = sem("o_summed")
        o_copied = sem("o_copied")
        o_stored = [sem(f"o_stored{i}") for i in range(2)]

        def unit0(b, c):
            return b * UB + c * NG

        def unit1(b, c):
            return b * UB + c * NG + UL

        def bank0(b, c):
            return b * BL + c * NM

        def part(r):
            return slice(r * CW, (r + 1) * CW)

        LAST = UK - 1

        block = ctx.enter_context(nc.Block())

        @block.sync
        def _(sp):
            def load_x_part(g, r):
                if g > 0 and r < LAST:
                    sp.wait_ge(x_part_lo_done, (g - 1) * LAST + r + 1)
                elif g > 0:
                    sp.wait_ge(x_lo_done, g)
                sp.dma_start(x_in[:, part(r)], x_units[0, g, :, part(r)]
                             ).then_inc(x_part_loaded[r] if r < LAST else x_loaded, 16)

            def load_first_w_part(r):
                sp.dma_start(w_in[0][:, part(r)], base_units[0, 0, :, part(r)]
                             ).then_inc(w_part_loaded[r] if r < LAST else w_loaded[0], 16)

            def load_x(b, g):
                sp.wait_ge(x_lo_done, b * NG + g)
                sp.dma_start(x_in[:, :], x_units[bass.ds(b, 1), bass.ds(g, 1)].rearrange("b g p e -> (b g p) e")
                             ).then_inc(x_loaded, 16)

            def load_a(b, lora, first=False):
                if not first:
                    sp.wait_ge(a_lo_done, b)
                sp.dma_start(a_in[:, :, :].rearrange("p k r -> p (k r)"),
                             lora_a_cols[bass.ds(lora, 1)].rearrange("l p e -> (l p) e")).then_inc(a_loaded, 16)

            def load_b(b, c, lora, first=False):
                if not first:
                    sp.wait_ge(b_lo_done, b * NC + c)
                sp.dma_start(b_in[:, :], lora_b_rows[bass.ds(lora, 1), :, bass.ds(c * CW, CW)].broadcast_to(
                    [P // RANK, RANK, CW])).then_inc(b_loaded, 16)

            def load_unit(u, g, src, first=False):
                if not first:
                    sp.wait_ge(w_lo_done, u + g - 1)
                sp.dma_start(w_in[g % 2][:, :], src).then_inc(w_loaded[g % 2], 16)

            def layer0_unit(c, g):
                return base_units[bass.ds(c, 1), g].rearrange("c p e -> (c p) e")

            def layer1_unit(weight, c, g):
                return weight_units[bass.ds(weight, 1), bass.ds(c, 1), g].rearrange("w c p e -> (w c p) e")

            for r in range(UK):
                load_x_part(0, r)
                load_first_w_part(r)
            load_unit(0, 1, layer0_unit(0, 1), first=True)
            for r in range(UK):
                load_x_part(1, r)
            load_unit(0, 2, layer0_unit(0, 2))
            for r in range(UK):
                load_x_part(2, r)
            sp.wait_ge(ids_loaded, 32)
            lora = sp.value_load(ids[0:1, 0:1], min_val=0, max_val=N_LORA - 1)
            load_a(0, lora, first=True)
            for r in range(UK):
                load_x_part(3, r)
            load_b(0, 0, lora, first=True)
            load_unit(0, 3, layer0_unit(0, 3))
            with sp.Fori(1, NC) as c:
                load_b(0, c, lora)
                for g in range(NG):
                    load_unit(unit0(0, c), g, layer0_unit(c, g))

            with sp.Fori(1, NB) as b:
                lora_b = sp.value_load(ids[0:1, bass.ds(b, 1)], min_val=0, max_val=N_LORA - 1)
                weight = sp.value_load(ids[0:1, bass.ds(b + (NB - 1), 1)], min_val=0, max_val=N_WEIGHT - 1)
                load_a(b, lora_b)
                with sp.Fori(0, NC) as c:
                    for g in range(NG):
                        load_unit(unit1(b - 1, c), g, layer1_unit(weight, c, g))
                        if g == 1:
                            load_x(b, c)
                with sp.Fori(0, NC) as c:
                    load_b(b, c, lora_b)
                    for g in range(NG):
                        load_unit(unit0(b, c), g, layer0_unit(c, g))

            weight = sp.value_load(ids[0:1, 2 * NB - 1:2 * NB], min_val=0, max_val=N_WEIGHT - 1)
            with sp.Fori(0, NC) as c:
                for g in range(NG):
                    load_unit(unit1(NB - 1, c), g, layer1_unit(weight, c, g))

        @block.gpsimd
        def _(pool):
            nc.gpsimd.memset(strip[:, 0:(NG - 1) * P], 0.0).then_inc(strip_zeroed, 1)
            nc.gpsimd.memset(strip[:, NG * P:], 0.0).then_inc(strip_zeroed, 1)
            pool.wait_ge(ident_loaded, 16)
            pool.wait_ge(strip_zeroed, 2)
            for r in range(UK):
                pool.wait_ge(w_part_loaded[r] if r < LAST else w_loaded[0], 16)
                diagonal = w_in[0][:, r * (CW + P):r * (CW + P) + P]
                nc.gpsimd.tensor_tensor(diagonal, diagonal, strip[:, (NG - 1) * P:NG * P], ALU.add
                                        ).then_inc(w_part_plus_i if r < LAST else w_plus_i, 1)

            def add_identity(u, c, g):
                pool.wait_ge(w_loaded[g % 2], (u // 2) * 16 + (g // 2 + 1) * 16)
                w = w_in[g % 2][:, :]
                diagonal = bass.AP(w.tensor, w.offset, [w.ap[0], [CW + P, UK], [1, P]])
                block_of_strip = strip[:, bass.ds((c + (NG - 1 - g)) * P, P)].unsqueeze(1).broadcast_to([P, UK, P])
                nc.gpsimd.tensor_tensor(diagonal, diagonal, block_of_strip, ALU.add).then_inc(w_plus_i, 1)

            for g in range(1, NG):
                add_identity(0, 0, g)
            with pool.Fori(1, NC) as c:
                for g in range(NG):
                    add_identity(unit0(0, c), c, g)
            with pool.Fori(0, NC) as c:
                for g in range(NG):
                    add_identity(unit1(0, c), c, g)
            with pool.Fori(1, NB) as b:
                with pool.Fori(0, NC) as c:
                    for g in range(NG):
                        add_identity(unit0(b, c), c, g)
                with pool.Fori(0, NC) as c:
                    for g in range(NG):
                        add_identity(unit1(b, c), c, g)

        @block.scalar
        def _(act):
            def split_x_part(g, r):
                act.wait_ge(x_part_loaded[r] if r < LAST else x_loaded, 16 * (g + 1))
                nc.scalar.copy(x_hi[:, g * UK + r, :], x_in[:, part(r)]
                               ).then_inc(x_part_hi_done if r < LAST else x_hi_done, 1)

            def split_first_w_part(r):
                if r < LAST:
                    act.wait_ge(w_part_plus_i, r + 1)
                else:
                    act.wait_ge(w_plus_i, 1)
                nc.scalar.copy(w_hi[0][:, r, :], w_in[0][:, part(r)]
                               ).then_inc(w_part_hi_done if r < LAST else w_hi_done, 1)

            def split_unit(u, g, first=False):
                act.wait_ge(w_plus_i, u + g + 1)
                if not first:
                    act.wait_ge(w_used, u + g - 1)
                nc.scalar.copy(w_hi[g % 2][:, :, :].rearrange("p k o -> p (k o)"), w_in[g % 2][:, :]
                               ).then_inc(w_hi_done, 1)

            def split_x(b, g, last_use):
                act.wait_ge(x_loaded, (b * NG + g + 1) * 16)
                act.wait_ge(w_used, last_use)
                nc.scalar.copy(x_hi[:, bass.ds(g * UK, UK), :].rearrange("p k s -> p (k s)"), x_in[:, :]
                               ).then_inc(x_hi_done, 1)

            def split_a(b, first=False):
                act.wait_ge(a_loaded, (b + 1) * 16)
                if not first:
                    act.wait_ge(h_summed, b)
                nc.scalar.copy(a_cols[:, :, :, 0:RANK],
                               a_in[:, :, :].unsqueeze(2).broadcast_to([P, KT, REP, RANK])).then_inc(a_hi_done, 1)

            def split_b(b, c, first=False):
                act.wait_ge(b_loaded, (b * NC + c + 1) * 16)
                if not first:
                    act.wait_ge(y_summed, bank0(b, c))
                nc.scalar.copy(b_rows[:, :], b_in[:, :]).then_inc(b_hi_done, 1)

            def split_h(b):
                act.wait_ge(h_summed, b + 1)
                nc.scalar.copy(h_rows[:, :], h_ps[:, :]).then_inc(h_hi_done, 1)

            def layer0_chunk(b, c):
                u = unit0(b, c)
                split_unit(u, 1)
                split_b(b, c)
                split_unit(u, 2)
                split_unit(u, 3)
                split_unit(u, 4)
                make_y(b, c)

            def make_y(b, c):
                for m in range(NM):
                    act.wait_ge(y_summed, bank0(b, c) + m + 1)
                    nc.scalar.activation(y_hi[:, bass.ds(c * NM + m, 1), :].rearrange("p k s -> p (k s)"),
                                         y_ps[m][:, :], ACT.Identity, bias=bias[:, bass.ds(c * NM + m, 1)]
                                         ).then_inc(y_hi_done, 1)

            def layer1_chunk(b, c, next_x, last=False):
                u = unit1(b, c)
                split_unit(u, 1)
                if next_x:
                    split_x(b + 1, c, unit1(b, 0))
                split_unit(u, 2)
                split_unit(u, 3)
                if not last:
                    split_unit(u, 4)
                for m in range(NM):
                    n = bank0(b, c) + m
                    act.wait_ge(o_copied, n + 1)
                    act.dma_start(out[bass.ds(b, 1), m * P:(m + 1) * P, bass.ds(c * CW, CW)].rearrange(
                        "b s o -> (b s) o"), o_st[m % 2][:, :]).then_inc(o_stored[m % 2], 16)

            act.dma_start(strip[:, (NG - 1) * P:NG * P], ident).then_inc(ident_loaded, 16)
            act.dma_start(ids[0:1, 0:NB], ids_lora).then_inc(ids_loaded, 16)
            act.dma_start(ids[0:1, NB:2 * NB], ids_weight).then_inc(ids_loaded, 16)
            act.dma_start(bias[:, :], bias_cols).then_inc(bias_loaded, 16)
            for r in range(UK):
                split_x_part(0, r)
                split_first_w_part(r)
            for r in range(UK):
                split_x_part(1, r)
            split_unit(0, 1, first=True)
            for r in range(UK):
                split_x_part(2, r)
            split_unit(0, 2)
            split_a(0, first=True)
            for r in range(UK):
                split_x_part(3, r)
            split_b(0, 0, first=True)
            split_unit(0, 3)
            split_h(0)
            split_unit(0, 4)
            act.wait_ge(bias_loaded, 16)
            make_y(0, 0)
            with act.Fori(1, NC) as c:
                layer0_chunk(0, c)
            with act.Fori(1, NB) as b:
                split_a(b)
                with act.Fori(0, NC) as c:
                    layer1_chunk(b - 1, c, True)
                split_h(b)
                with act.Fori(0, NC) as c:
                    layer0_chunk(b, c)
            with act.Fori(0, NC - 1) as c:
                layer1_chunk(NB - 1, c, False)
            layer1_chunk(NB - 1, NC - 1, False, last=True)
            for i in range(2):
                act.wait_ge(o_stored[i], 16 * NB * BL // 2)

        @block.vector
        def _(dve):
            def split_x_part(g, r):
                if r < LAST:
                    dve.wait_ge(x_part_hi_done, g * LAST + r + 1)
                else:
                    dve.wait_ge(x_hi_done, g + 1)
                k = g * UK + r
                nc.vector.tensor_tensor(x_lo[:, k, :], x_in[:, part(r)], x_hi[:, k, :].bitcast(F32), ALU.subtract
                                        ).then_inc(x_part_lo_done if r < LAST else x_lo_done, 1)

            def split_first_w_part(r):
                if r < LAST:
                    dve.wait_ge(w_part_hi_done, r + 1)
                else:
                    dve.wait_ge(w_hi_done, 1)
                nc.vector.tensor_tensor(w_lo[0][:, r, :], w_in[0][:, part(r)], w_hi[0][:, r, :].bitcast(F32),
                                        ALU.subtract).then_inc(w_part_lo_done if r < LAST else w_lo_done, 1)

            def split_unit(u, g):
                dve.wait_ge(w_hi_done, u + g + 1)
                flat = "p k o -> p (k o)"
                nc.vector.tensor_tensor(w_lo[g % 2][:, :, :].rearrange(flat), w_in[g % 2][:, :],
                                        w_hi[g % 2][:, :, :].rearrange(flat).bitcast(F32), ALU.subtract
                                        ).then_inc(w_lo_done, 1)

            def split_x(b, g):
                dve.wait_ge(x_hi_done, b * NG + g + 1)
                flat = "p k s -> p (k s)"
                nc.vector.tensor_tensor(x_lo[:, bass.ds(g * UK, UK), :].rearrange(flat), x_in[:, :],
                                        x_hi[:, bass.ds(g * UK, UK), :].rearrange(flat).bitcast(F32), ALU.subtract
                                        ).then_inc(x_lo_done, 1)

            def split_a(b):
                dve.wait_ge(a_hi_done, b + 1)
                nc.vector.tensor_tensor(a_cols[:, :, :, RANK:2 * RANK],
                                        a_in[:, :, :].unsqueeze(2).broadcast_to([P, KT, REP, RANK]),
                                        a_cols[:, :, :, 0:RANK].bitcast(F32), ALU.subtract).then_inc(a_lo_done, 1)

            def split_b(b, c):
                dve.wait_ge(b_hi_done, b * NC + c + 1)
                nc.vector.tensor_tensor(b_rows[P // 2:P, :], b_in[P // 2:P, :], b_rows[P // 2:P, :].bitcast(F32),
                                        ALU.subtract).then_inc(b_lo_done, 1)

            def split_h(b):
                dve.wait_ge(h_hi_done, b + 1)
                for q in (1, 3):
                    rows = slice(q * Q, (q + 1) * Q)
                    nc.vector.tensor_tensor(h_rows[rows, :], h_ps[rows, :], h_rows[rows, :].bitcast(F32),
                                            ALU.subtract).then_inc(h_lo_done, 1)

            def layer0_chunk(b, c):
                u = unit0(b, c)
                split_unit(u, 1)
                split_b(b, c)
                split_unit(u, 2)
                split_unit(u, 3)
                split_unit(u, 4)
                make_y(b, c)

            def make_y(b, c):
                for m in range(NM):
                    dve.wait_ge(y_hi_done, bank0(b, c) + m + 1)
                    k = bass.ds(c * NM + m, 1)
                    flat = "p k s -> p (k s)"
                    nc.vector.scalar_tensor_tensor(y_lo[:, k, :].rearrange(flat), y_ps[m][:, :], bias[:, k],
                                                   y_hi[:, k, :].rearrange(flat).bitcast(F32), ALU.add, ALU.subtract
                                                   ).then_inc(y_lo_done, 1)

            def layer1_chunk(b, c, next_x, last=False, first=False):
                u = unit1(b, c)
                split_unit(u, 1)
                if next_x:
                    split_x(b + 1, c)
                split_unit(u, 2)
                split_unit(u, 3)
                if not last:
                    split_unit(u, 4)
                for m in range(NM):
                    n = bank0(b, c) + m
                    if m < NM - 1:
                        dve.wait_ge(o_summed, (b * NC + c) * (NM - 1) + m + 1)
                    else:
                        dve.wait_ge(w_used, u + NG)
                    if not (first and m < 2):
                        dve.wait_ge(o_stored[m % 2], (bank0(b, c) // 2 + m // 2) * 16)
                    nc.vector.tensor_copy(o_st[m % 2][:, :], o_ps[m][:, :]).then_inc(o_copied, 1)

            for r in range(UK):
                split_x_part(0, r)
                split_first_w_part(r)
            for r in range(UK):
                split_x_part(1, r)
            split_unit(0, 1)
            for r in range(UK):
                split_x_part(2, r)
            split_unit(0, 2)
            split_a(0)
            for r in range(UK):
                split_x_part(3, r)
            split_b(0, 0)
            split_unit(0, 3)
            split_h(0)
            split_unit(0, 4)
            dve.wait_ge(bias_loaded, 16)
            make_y(0, 0)
            with dve.Fori(1, NC) as c:
                layer0_chunk(0, c)
            split_a(1)
            layer1_chunk(0, 0, True, first=True)
            with dve.Fori(1, NC) as c:
                layer1_chunk(0, c, True)
            with dve.Fori(1, NB - 1) as b:
                split_h(b)
                with dve.Fori(0, NC) as c:
                    layer0_chunk(b, c)
                split_a(b + 1)
                with dve.Fori(0, NC) as c:
                    layer1_chunk(b, c, True)
            split_h(NB - 1)
            with dve.Fori(0, NC) as c:
                layer0_chunk(NB - 1, c)
            with dve.Fori(0, NC - 1) as c:
                layer1_chunk(NB - 1, c, False)
            layer1_chunk(NB - 1, NC - 1, False, last=True)

        @block.tensor
        def _(pe):
            def make_h(b, first=False):
                if not first:
                    pe.wait_ge(o_copied, bank0(b - 1, NC - 1) + 1)
                pe.wait_ge(a_hi_done, b + 1)
                pe.wait_ge(a_lo_done, b + 1)
                for k in range(KT):
                    if k % UK == 0:
                        pe.wait_ge(x_hi_done, b * NG + k // UK + 1)
                        pe.wait_ge(x_lo_done, b * NG + k // UK + 1)
                    a = a_cols[:, k, :, :].rearrange("p q r -> p (q r)")
                    nc.tensor.matmul(h_ps[:, :], a, x_hi[:, k, :], start=(k == 0), stop=False)
                    mm = nc.tensor.matmul(h_ps[:, :], a, x_lo[:, k, :], start=False, stop=(k == KT - 1))
                mm.then_inc(h_summed, 1)

            def wait_unit(u, g):
                pe.wait_ge(w_hi_done, u + g + 1)
                pe.wait_ge(w_lo_done, u + g + 1)

            def wait_first_x(g, r):
                if r < LAST:
                    pe.wait_ge(x_part_hi_done, g * LAST + r + 1)
                    pe.wait_ge(x_part_lo_done, g * LAST + r + 1)
                else:
                    pe.wait_ge(x_hi_done, g + 1)
                    pe.wait_ge(x_lo_done, g + 1)

            def first_unit():
                for r in range(UK):
                    wait_first_x(0, r)
                    pe.wait_ge(w_part_hi_done if r < LAST else w_hi_done, r + 1 if r < LAST else 1)
                    pe.wait_ge(w_part_lo_done if r < LAST else w_lo_done, r + 1 if r < LAST else 1)
                    for m in range(NM):
                        o = slice(m * P, (m + 1) * P)
                        nc.tensor.matmul(y_ps[m][:, :], w_hi[0][:, r, o], x_hi[:, r, :], start=(r == 0), stop=False)
                        nc.tensor.matmul(y_ps[m][:, :], w_hi[0][:, r, o], x_lo[:, r, :], start=False, stop=False)
                        mm = nc.tensor.matmul(y_ps[m][:, :], w_lo[0][:, r, o], x_hi[:, r, :], start=False, stop=False)
                mm.then_inc(w_used, 1)

            def layer0_chunk(b, c, first=False):
                if first:
                    first_unit()
                for g in range(1 if first else 0, NG):
                    if first:
                        for r in range(UK):
                            wait_first_x(g, r)
                        if g == NG - 1:
                            make_h(b, first=True)
                    wait_unit(unit0(b, c), g)
                    wh, wl = w_hi[g % 2], w_lo[g % 2]
                    for m in range(NM):
                        if g == 0 and not first:
                            pe.wait_ge(y_lo_done, bank0(b, c) - NM + m + 1)
                        o = slice(m * P, (m + 1) * P)
                        for r in range(UK):
                            k = g * UK + r
                            nc.tensor.matmul(y_ps[m][:, :], wh[:, r, o], x_hi[:, k, :], start=(k == 0), stop=False)
                            nc.tensor.matmul(y_ps[m][:, :], wh[:, r, o], x_lo[:, k, :], start=False, stop=False)
                            mm = nc.tensor.matmul(y_ps[m][:, :], wl[:, r, o], x_hi[:, k, :], start=False, stop=False)
                        if g == NG - 1:
                            if m == 0:
                                pe.wait_ge(h_hi_done, b + 1)
                                pe.wait_ge(h_lo_done, (b + 1) * 2)
                                pe.wait_ge(b_hi_done, b * NC + c + 1)
                                pe.wait_ge(b_lo_done, b * NC + c + 1)
                            nc.tensor.matmul(y_ps[m][:, :], b_rows[:, o], h_rows[:, :], start=False, stop=True
                                             ).then_inc(y_summed, 1)
                    mm.then_inc(w_used, 1)

            def layer1_chunk(b, c, first=False):
                for g in range(NG):
                    wait_unit(unit1(b, c), g)
                    pe.wait_ge(y_hi_done, bank0(b, 0) + (g + 1) * NM)
                    pe.wait_ge(y_lo_done, bank0(b, 0) + (g + 1) * NM)
                    wh, wl = w_hi[g % 2], w_lo[g % 2]
                    for m in range(NM):
                        if g == 0 and not first:
                            pe.wait_ge(o_copied, bank0(b, c) - NM + m + 1)
                        s = slice(m * P, (m + 1) * P)
                        for r in range(UK):
                            k = g * UK + r
                            nc.tensor.matmul(o_ps[m][:, :], y_hi[:, k, s], wh[:, r, :], start=(k == 0), stop=False)
                            nc.tensor.matmul(o_ps[m][:, :], y_hi[:, k, s], wl[:, r, :], start=False, stop=False)
                            mm = nc.tensor.matmul(o_ps[m][:, :], y_lo[:, k, s], wh[:, r, :], start=False,
                                                  stop=(k == KT - 1))
                        if g == NG - 1 and m < NM - 1:
                            mm.then_inc(o_summed, 1)
                    mm.then_inc(w_used, 1)

            layer0_chunk(0, 0, first=True)
            with pe.Fori(1, NC) as c:
                layer0_chunk(0, c)
            layer1_chunk(0, 0, first=True)
            with pe.Fori(1, NC) as c:
                layer1_chunk(0, c)
            with pe.Fori(1, NB) as b:
                make_h(b)
                with pe.Fori(0, NC) as c:
                    layer0_chunk(b, c)
                with pe.Fori(0, NC) as c:
                    layer1_chunk(b, c)


def kernel(**inputs):
    import numpy as np
    import concourse.bacc as bacc
    from concourse.bass_utils import run_bass_kernel_spmd

    a = {name: np.asarray(value) for name, value in inputs.items()}
    x, base, weight = a["x"], a["L0_cond_base_weight"], a["L1_cond_weight"]
    lora_a, lora_b = a["L0_cond_lora_A_w"], a["L0_cond_lora_B_w"]
    nb, s, d = x.shape
    ng, nc_, kt = d // (P * UK), d // CW, d // P

    def weight_layout(w):
        w = w.reshape(*w.shape[:-2], nc_, CW, ng, UK, P)
        n = w.ndim
        w = w.transpose(*range(n - 5), n - 5, n - 3, n - 1, n - 2, n - 4)
        return np.ascontiguousarray(w).reshape(*w.shape[:-2], UK * CW)

    arrays = {
        "x_units": np.ascontiguousarray(x.reshape(nb, s, ng, UK, P).transpose(0, 2, 4, 3, 1)).reshape(nb, ng, P, UK * s),
        "ids_lora": a["itok_B_6_15"].reshape(1, nb),
        "ids_weight": a["itok_B_3_7"].reshape(1, nb),
        "base_units": weight_layout(base),
        "bias_cols": np.ascontiguousarray(a["L0_cond_base_bias"].reshape(kt, P).T),
        "lora_a_cols": np.ascontiguousarray(lora_a.reshape(*lora_a.shape[:2], kt, P).transpose(0, 3, 2, 1)).reshape(
            lora_a.shape[0], P, -1),
        "lora_b_rows": np.ascontiguousarray(lora_b.transpose(0, 2, 1)),
        "weight_units": weight_layout(weight),
        "ident": np.eye(P, dtype=np.float32),
    }
    nc = bacc.Bacc("TRN2", target_bir_lowering=False, num_devices=1)
    args = [nc.dram_tensor(f"in_{k}", v.shape, mybir.dt.from_np(v.dtype), kind="ExternalInput").ap()
            for k, v in arrays.items()]
    out = nc.dram_tensor("out_y", (nb, s, d), F32, kind="ExternalOutput").ap()
    cond_resid_kernel(nc, *args, out)
    r = run_bass_kernel_spmd(nc, [{f"in_{k}": v for k, v in arrays.items()}], core_ids=[0])
    return r.results[0]["out_y"]
```
